# Optimizing a Trainium2 kernel written in Bass

```python
import numpy as np
import jax
import jax.numpy as jnp

def _softmax(x, axis=-1):
    return jax.nn.softmax(x, axis=axis)

def _gelu(x):
    return jax.nn.gelu(x, approximate=True)

def _silu(x):
    return jax.nn.silu(x)

def _sigmoid(x):
    return jax.nn.sigmoid(x)

def _layernorm(x, axis=-1, eps=1e-05):
    m = jnp.mean(x, axis=axis, keepdims=True)
    v = jnp.var(x, axis=axis, keepdims=True)
    return (x - m) / jnp.sqrt(v + eps)

def _scatter_add(tgt, idx, src, axis=0):
    return tgt.at[idx].add(src)

def _segment_sum(src, seg, n):
    return jax.ops.segment_sum(src, seg, n)
kernel_name = 'mk_adj_resnorm_d1_adj_r2_907d80'

def setup_inputs(seed: int=0):
    np.random.seed(seed)
    _w = jnp.asarray

    def _rec_inputs():
        import jax
        import jax.numpy as jnp
        _gk = jax.random.key(seed)
        x = -0.000929 + 1 * jax.random.normal(jax.random.fold_in(_gk, 1), (8192, 64), jnp.float32)
        _w = (1.0 + jnp.arange(8192, dtype=jnp.float32)) ** (-0.5)
        _w = _w / _w.mean()
        _pij = jnp.clip(0.000244141 * _w[:, None] * _w[None, :], 0.0, 1.0)
        _a = jax.random.uniform(jax.random.fold_in(_gk, 2), (8192, 8192)) < _pij
        _a = jnp.logical_or(_a, jnp.eye(8192, dtype=bool))
        _af = _a.astype(jnp.float32)
        _af = _af * jax.random.uniform(jax.random.fold_in(_gk, 3), (8192, 8192), jnp.float32, 0.05, 1)
        adj = _af
        return (x, adj)
    x, adj = _rec_inputs()

    def _L0_gnn_setup():
        import jax, jax.numpy as jnp
        import numpy as np
        P_DROP = 0.1
        key = jax.random.key(seed)
        k1, k2, k3 = jax.random.split(key, 3)
        N, D = (8192, 64)
        x = jax.random.normal(k1, (N, D), dtype=jnp.float32)
        adj = jax.random.uniform(k2, (N, N), dtype=jnp.float32)
        u = jax.random.uniform(k3, (N, D), dtype=jnp.float32)
        return {'x': x, 'adj': adj, 'u': u}
    _L0_gnn_all = _L0_gnn_setup()
    _L0_gnn_in = {k: v for k, v in _L0_gnn_all.items() if k in ('u',)}
    del _L0_gnn_all
    return {'x': x, 'adj': adj, 'L0_gnn_u': _L0_gnn_in['u']}

def reference(x, adj, L0_gnn_u):
    import jax
    import jax.numpy as jnp

    def _L0_gnn_ref(x, adj, u):
        import jax, jax.numpy as jnp
        import numpy as np
        P_DROP = 0.1
        keep = (u >= P_DROP).astype(x.dtype)
        x_drop = x * keep / (1.0 - P_DROP)
        return jnp.matmul(adj, x_drop)
    x = _layernorm(x + _L0_gnn_ref(x, adj, L0_gnn_u), axis=-1)
    return x

_drawn_inputs = setup_inputs


def setup_inputs(seed=0):
    import zlib

    import numpy as np

    out = dict(_drawn_inputs(seed))
    spreads = {}
    factors = {}
    for name, (base, spread) in spreads.items():
        noise = np.random.default_rng([zlib.crc32(name.encode()), seed]).standard_normal(out[name].shape)
        drawn = base * np.exp(spread * noise) if base else spread * noise
        out[name] = jnp.asarray(drawn.astype(out[name].dtype))
    for name, factor in factors.items():
        out[name] = (out[name] * factor).astype(out[name].dtype)
    return out
```

```python
import concourse.bass as bass
from concourse import mybir
from contextlib import ExitStack

N = 8192
D = 64
P = 128
NB = N // P
COLS = 512
CHUNKS = N // COLS
J = COLS // P
SLOTS = 8
PB = NB // SLOTS
XQ = 4
XB = NB // XQ
P_DROP = 0.1
EPS = 1e-5


def graph_layernorm(nc, x, adj, u, out):
    fp32 = mybir.dt.float32
    ALU = mybir.AluOpType
    ACT = mybir.ActivationFunctionType
    AX_X = mybir.AxisListType.X

    ctx = ExitStack()
    with ctx:
        def sb(name, shape):
            return ctx.enter_context(nc.sbuf_tensor(name, shape, fp32))

        def pb(name, shape):
            return ctx.enter_context(nc.psum_tensor(name, shape, fp32))

        def sem(name):
            return ctx.enter_context(nc.semaphore(name))

        pieces = [sb(f"piece{s}", [P, PB, COLS]) for s in range(SLOTS)]
        x_sb = sb("x_sb", [P, NB, D])
        u_sb = sb("u_sb", [P, NB, D])
        xdrop = sb("xdrop", [P, NB, D])
        fold = sb("fold", [P, D])
        eps = sb("eps", [P, 1])
        sums_T = sb("sums_T", [P, 2, COLS])
        y = sb("y", [P, 2, J, D])
        row_sum = sb("row_sum", [P, J])
        centered = sb("centered", [P, J, D])
        squares = sb("squares", [P, J, D])
        square_sum = sb("square_sum", [P, J])
        std = sb("std", [P, J])
        rstd = sb("rstd", [P, J])
        rows = sb("rows", [P, 2, J, D])
        acc = [pb(f"acc{i}", [P, COLS]) for i in range(2)]
        folded = [pb(f"folded{i}", [P, J, D]) for i in range(2)]

        piece_in = [sem(f"piece_in{s}") for s in range(SLOTS)]
        x_in = [sem(f"x_in{q}") for q in range(XQ)]
        piece_used = sem("piece_used")
        sums_copied = sem("sums_copied")
        folded_ready = sem("folded_ready")
        y_ready = sem("y_ready")
        dropped = sem("dropped")
        fold_zero = sem("fold_zero")
        fold_half = sem("fold_half")
        fold_ready = sem("fold_ready")
        eps_ready = sem("eps_ready")
        sum_ready = sem("sum_ready")
        centered_ready = sem("centered_ready")
        squares_ready = sem("squares_ready")
        var_ready = sem("var_ready")
        std_ready = sem("std_ready")
        rstd_ready = sem("rstd_ready")
        rows_ready = sem("rows_ready")
        stored = [sem(f"stored{i}") for i in range(2)]

        block = ctx.enter_context(nc.Block())

        @block.sync
        def _(sp):
            def load(c, s, used=None):
                if used is not None:
                    sp.wait_ge(piece_used, used)
                sp.dma_start(pieces[s][:, :, :], adj[c * SLOTS + s, :, :, :]).then_inc(piece_in[s], 16)

            for s in range(SLOTS):
                load(0, s)
            with sp.Fori(1, CHUNKS) as c:
                for s in range(SLOTS):
                    load(c, s, c * SLOTS + (s + 1 - SLOTS))

        @block.gpsimd
        def _(pool):
            nc.gpsimd.memset(eps[:, :], EPS).then_inc(eps_ready, 1)
            nc.gpsimd.memset(fold[:, :], 0.0).then_inc(fold_zero, 1)
            pool.wait_ge(fold_zero, 1)
            nc.gpsimd.affine_select(out=fold[:, :], in_=fold[:, :], compare_op=ALU.not_equal, fill=1.0, base=0,
                                    pattern=[[-1, D]], channel_multiplier=1).then_inc(fold_half, 1)
            pool.wait_ge(fold_half, 1)
            nc.gpsimd.affine_select(out=fold[:, :], in_=fold[:, :], compare_op=ALU.not_equal, fill=1.0, base=-D,
                                    pattern=[[-1, D]], channel_multiplier=1).then_inc(fold_ready, 1)

        @block.tensor
        def _(pe):
            def multiply(c, i, s, first=False):
                pe.wait_ge(piece_in[s], 16 * c + 16)
                if first and s % (SLOTS // XQ) == 0:
                    pe.wait_ge(dropped, s // (SLOTS // XQ) + 1)
                for b in range(PB):
                    k = s * PB + b
                    h = b % 2
                    last = nc.tensor.matmul(acc[i][D * h:D * h + D, :], xdrop[:, k, :], pieces[s][:, b, :],
                                            start=(k < 2), stop=(k >= NB - 2))
                last.then_inc(piece_used, 1)

            def fold_rows(c, i, wait_free=True):
                pe.wait_ge(sums_copied, c + 1)
                if wait_free:
                    pe.wait_ge(y_ready, c - 1)
                for j in range(J):
                    last = nc.tensor.matmul(folded[i][:, j, :], sums_T[:, i, j * P:j * P + P], fold[:, :],
                                            start=True, stop=True)
                last.then_inc(folded_ready, 1)

            for s in range(SLOTS):
                multiply(0, 0, s, first=True)
            pe.wait_ge(fold_ready, 1)
            multiply(1, 1, 0)
            fold_rows(0, 0, wait_free=False)
            for s in range(1, SLOTS):
                multiply(1, 1, s)
            with pe.Fori(1, CHUNKS // 2) as t:
                for i in range(2):
                    c = t * 2 + i
                    pe.wait_ge(sums_copied, c - 1)
                    multiply(c, i, 0)
                    if i == 0:
                        fold_rows(c - 1, 1)
                    else:
                        fold_rows(c - 1, 0)
                    for s in range(1, SLOTS):
                        multiply(c, i, s)
            fold_rows(CHUNKS - 1, 1)

        @block.scalar
        def _(act):
            for q in range(XQ):
                for dst, src in ((x_sb, x), (u_sb, u)):
                    act.dma_start(dst[:, q * XB:q * XB + XB, :], src[:, q * XB:q * XB + XB, :]).then_inc(x_in[q], 16)
            act.wait_ge(eps_ready, 1)

            def step(c, i, again=True):
                act.wait_ge(piece_used, c * SLOTS + SLOTS)
                if again:
                    act.wait_ge(folded_ready, c - 1)
                nc.scalar.copy(sums_T[:, i, :], acc[i][:, :]).then_inc(sums_copied, 1)
                act.wait_ge(var_ready, c + 1)
                nc.scalar.activation(std[:, :], square_sum[:, :], ACT.Sqrt, bias=eps[:, :], scale=1.0 / D).then_inc(std_ready, 1)
                act.wait_ge(rows_ready, c + 1)
                act.dma_start(out[:, bass.ds(J * c, J), :], rows[:, i, :, :]).then_inc(stored[i], 16)

            step(0, 0, again=False)
            step(1, 1, again=False)
            with act.Fori(1, CHUNKS // 2) as t:
                for i in range(2):
                    step(t * 2 + i, i)
            for i in range(2):
                act.wait_ge(stored[i], 16 * (CHUNKS // 2))

        @block.vector
        def _(dve):
            for q in range(XQ):
                sl = slice(q * XB, q * XB + XB)
                dve.wait_ge(x_in[q], 32)
                nc.vector.scalar_tensor_tensor(out=xdrop[:, sl, :], in0=u_sb[:, sl, :], scalar=P_DROP, in1=x_sb[:, sl, :],
                                               op0=ALU.is_ge, op1=ALU.mult).then_inc(dropped, 1)

            def per_row(v):
                return v[:, :].unsqueeze(2).to_broadcast([P, J, D])

            def normalise(c, i, stores=None):
                dve.wait_ge(folded_ready, c + 1)
                nc.vector.scalar_tensor_tensor(out=y[:, i, :, :], in0=folded[i][:, :, :], scalar=1.0 / (1.0 - P_DROP),
                                               in1=x_sb[:, bass.ds(J * c, J), :],
                                               op0=ALU.mult, op1=ALU.add).then_inc(y_ready, 1)
                dve.wait_ge(y_ready, c + 1)
                nc.vector.reduce_sum(row_sum[:, :], y[:, i, :, :], AX_X).then_inc(sum_ready, 1)
                dve.wait_ge(sum_ready, c + 1)
                nc.vector.scalar_tensor_tensor(out=centered[:, :, :], in0=per_row(row_sum), scalar=-1.0 / D,
                                               in1=y[:, i, :, :], op0=ALU.mult, op1=ALU.add).then_inc(centered_ready, 1)
                dve.wait_ge(centered_ready, c + 1)
                nc.vector.tensor_tensor(squares[:, :, :], centered[:, :, :], centered[:, :, :],
                                        ALU.mult).then_inc(squares_ready, 1)
                dve.wait_ge(squares_ready, c + 1)
                nc.vector.reduce_sum(square_sum[:, :], squares[:, :, :], AX_X).then_inc(var_ready, 1)
                dve.wait_ge(std_ready, c + 1)
                nc.vector.reciprocal(rstd[:, :], std[:, :]).then_inc(rstd_ready, 1)
                if stores is not None:
                    dve.wait_ge(stored[i], stores)
                dve.wait_ge(rstd_ready, c + 1)
                nc.vector.tensor_tensor(rows[:, i, :, :], centered[:, :, :], per_row(rstd),
                                        ALU.mult).then_inc(rows_ready, 1)
                dve.wait_ge(rows_ready, c + 1)

            normalise(0, 0)
            normalise(1, 1)
            with dve.Fori(1, CHUNKS // 2) as t:
                for i in range(2):
                    normalise(t * 2 + i, i, stores=t * 16)


def kernel(x, adj, L0_gnn_u):
    import numpy as np
    import concourse.bacc as bacc
    from concourse.bass_utils import run_bass_kernel_spmd

    nc = bacc.Bacc("TRN2", target_bir_lowering=False, num_devices=1)
    fp32 = mybir.dt.float32
    a = np.asarray(adj).reshape(P, CHUNKS, J, P, SLOTS, PB).transpose(1, 4, 3, 5, 2, 0)
    arrays = {
        "x": np.ascontiguousarray(x).reshape(P, NB, D),
        "adj": np.ascontiguousarray(a).reshape(CHUNKS * SLOTS, P, PB, COLS),
        "u": np.ascontiguousarray(L0_gnn_u).reshape(P, NB, D),
    }
    args = [nc.dram_tensor(n, v.shape, fp32, kind="ExternalInput").ap() for n, v in arrays.items()]
    out = nc.dram_tensor("out", (P, NB, D), fp32, kind="ExternalOutput").ap()
    graph_layernorm(nc, *args, out)
    r = run_bass_kernel_spmd(nc, [arrays], core_ids=[0])
    return r.results[0]["out"].reshape(N, D)
```

```python
import concourse.bass as bass
from concourse import mybir
from contextlib import ExitStack

N = 8192
D = 64
P = 128
NB = N // P
COLS = 512
CHUNKS = N // COLS
J = COLS // P
SLOTS = 16
PB = NB // SLOTS
NARROW = 2
LAST_J = J // NARROW
LAST_COLS = LAST_J * P
LAST_PB = PB * COLS // LAST_COLS
LAST_SLOTS = NB // LAST_PB
TAIL_PARTS = (4, 4)
FINAL = CHUNKS - 2 + NARROW
XQ = 4
XB = NB // XQ
P_DROP = 0.1
EPS = 1e-5


def graph_layernorm(nc, x, adj, adj_last, u, out):
    fp32 = mybir.dt.float32
    ALU = mybir.AluOpType
    ACT = mybir.ActivationFunctionType
    AX_X = mybir.AxisListType.X

    ctx = ExitStack()
    with ctx:
        def sb(name, shape):
            return ctx.enter_context(nc.sbuf_tensor(name, shape, fp32))

        def pb(name, shape):
            return ctx.enter_context(nc.psum_tensor(name, shape, fp32))

        def sem(name):
            return ctx.enter_context(nc.semaphore(name))

        pieces = [sb(f"piece{s}", [P, PB, COLS]) for s in range(SLOTS)]
        x_sb = sb("x_sb", [P, NB, D])
        u_sb = sb("u_sb", [P, NB, D])
        xdrop = sb("xdrop", [P, NB, D])
        node_sum = sb("node_sum", [P, 2, NB])
        fold = sb("fold", [P, D])
        eps = sb("eps", [P, 1])
        sums_T = sb("sums_T", [P, 2, COLS])
        y = sb("y", [P, 2, J, D])
        squares = sb("squares", [P, J, D])
        square_sum = sb("square_sum", [P, J])
        std = sb("std", [P, J])
        rstd = sb("rstd", [P, J])
        rows = sb("rows", [P, 2, J, D])
        acc = [pb(f"acc{i}", [P, COLS]) for i in range(2)]
        folded = [pb(f"folded{i}", [P, J, D]) for i in range(2)]

        last_parts = [(sum(TAIL_PARTS[:n]), TAIL_PARTS[n]) for n in range(len(TAIL_PARTS))]
        narrow = [piece[:, :, :].rearrange("p b i -> p (b i)").rearrange("p (b i) -> p b i", i=LAST_COLS)
                  for piece in pieces]

        part_in = [sem(f"part_in{n}") for n in range(len(TAIL_PARTS))]
        piece_in = [sem(f"piece_in{s}") for s in range(SLOTS)]
        x_in = [sem(f"x_in{q}") for q in range(XQ)]
        piece_used = sem("piece_used")
        sums_copied = sem("sums_copied")
        folded_ready = sem("folded_ready")
        y_ready = sem("y_ready")
        dropped = sem("dropped")
        fold_zero = sem("fold_zero")
        fold_half = sem("fold_half")
        fold_ready = sem("fold_ready")
        eps_ready = sem("eps_ready")
        masked = sem("masked")
        node_sum_ready = sem("node_sum_ready")
        x_centred = sem("x_centred")
        squares_ready = sem("squares_ready")
        var_ready = sem("var_ready")
        std_ready = sem("std_ready")
        rstd_ready = sem("rstd_ready")
        rows_ready = sem("rows_ready")
        stored = [sem(f"stored{i}") for i in range(2)]

        block = ctx.enter_context(nc.Block())

        @block.sync
        def _(sp):
            def load(c, s):
                sp.dma_start(pieces[s][:, :, :], adj[c * SLOTS + s, :, :, :]).then_inc(piece_in[s], 16)

            for s in range(SLOTS):
                load(0, s)
            with sp.Fori(1, CHUNKS - 1) as c:
                for s in range(SLOTS):
                    sp.wait_ge(piece_used, c * SLOTS + (s + 1 - SLOTS))
                    load(c, s)
            for s in range(SLOTS):
                sp.wait_ge(piece_used, (CHUNKS - 2) * SLOTS + s + 1)
                if s < SLOTS - 1:
                    sp.dma_start(narrow[s], adj_last[s, :, :, :]).then_inc(piece_in[s], 16)
                else:
                    for n, (b, size) in enumerate(last_parts):
                        sp.dma_start(narrow[s][:, b:b + size, :],
                                     adj_last[s, :, b:b + size, :]).then_inc(part_in[n], 16)

        @block.gpsimd
        def _(pool):
            nc.gpsimd.memset(eps[:, :], EPS).then_inc(eps_ready, 1)
            nc.gpsimd.memset(fold[:, :], 0.0).then_inc(fold_zero, 1)
            pool.wait_ge(fold_zero, 1)
            nc.gpsimd.affine_select(out=fold[:, :], in_=fold[:, :], compare_op=ALU.not_equal, fill=1.0, base=0,
                                    pattern=[[-1, D]], channel_multiplier=1).then_inc(fold_half, 1)
            pool.wait_ge(fold_half, 1)
            nc.gpsimd.affine_select(out=fold[:, :], in_=fold[:, :], compare_op=ALU.not_equal, fill=1.0, base=-D,
                                    pattern=[[-1, D]], channel_multiplier=1).then_inc(fold_ready, 1)

        @block.tensor
        def _(pe):
            def products(i, piece, k0, blocks, cols):
                for b in range(blocks):
                    k = k0 + b
                    h = b % 2
                    last = nc.tensor.matmul(acc[i][D * h:D * h + D, 0:cols], xdrop[:, k, :], piece[:, b, :],
                                            start=(k < 2), stop=(k >= NB - 2))
                last.then_inc(piece_used, 1)

            def multiply(c, i, s):
                pe.wait_ge(piece_in[s], c * 16 + 16)
                products(i, pieces[s], s * PB, PB, COLS)

            def fold_rows(c, i, nj=J):
                pe.wait_ge(sums_copied, c + 1)
                for j in range(nj):
                    last = nc.tensor.matmul(folded[i][:, j, :], sums_T[:, i, j * P:j * P + P], fold[:, :],
                                            start=True, stop=True)
                last.then_inc(folded_ready, 1)

            def wide(c, i):
                multiply(c, i, 0)
                fold_rows(c - 1, 1 - i)
                for s in range(1, SLOTS):
                    multiply(c, i, s)

            for s in range(SLOTS):
                if s % (SLOTS // XQ) == 0:
                    pe.wait_ge(dropped, s // (SLOTS // XQ) + 1)
                multiply(0, 0, s)
            pe.wait_ge(fold_ready, 1)
            wide(1, 1)
            with pe.Fori(1, (CHUNKS - 2) // 2) as t:
                for i in range(2):
                    c = t * 2 + i
                    pe.wait_ge(sums_copied, c - 1)
                    wide(c, i)
            pe.wait_ge(sums_copied, CHUNKS - 3)
            wide(CHUNKS - 2, 0)
            for m in range(NARROW):
                c = CHUNKS - 1 + m
                i = c % 2
                pe.wait_ge(sums_copied, c - 1)
                for n in range(LAST_SLOTS):
                    s = m * LAST_SLOTS + n
                    if s < SLOTS - 1:
                        pe.wait_ge(piece_in[s], 16 * CHUNKS)
                        products(i, narrow[s], n * LAST_PB, LAST_PB, LAST_COLS)
                    else:
                        for part, (b, size) in enumerate(last_parts):
                            pe.wait_ge(part_in[part], 16)
                            products(i, narrow[s][:, b:b + size, :], n * LAST_PB + b, size, LAST_COLS)
                    if n == 0:
                        fold_rows(c - 1, 1 - i, nj=LAST_J if m else J)
            fold_rows(FINAL, FINAL % 2, nj=LAST_J)

        @block.scalar
        def _(act):
            for q in range(XQ):
                for dst, src in ((x_sb, x), (u_sb, u)):
                    act.dma_start(dst[:, q * XB:q * XB + XB, :], src[:, q * XB:q * XB + XB, :]).then_inc(x_in[q], 16)
            act.wait_ge(eps_ready, 1)

            def step(c, i, used, block0, again=True, nj=J):
                act.wait_ge(piece_used, used)
                if again:
                    act.wait_ge(folded_ready, c - 1)
                nc.scalar.copy(sums_T[:, i, 0:nj * P], acc[i][:, 0:nj * P]).then_inc(sums_copied, 1)
                act.wait_ge(var_ready, c + 1)
                nc.scalar.activation(std[:, 0:nj], square_sum[:, 0:nj], ACT.Sqrt, bias=eps[:, :],
                                     scale=1.0 / D).then_inc(std_ready, 1)
                act.wait_ge(rows_ready, c + 1)
                act.dma_start(out[:, bass.ds(block0, nj), :], rows[:, i, 0:nj, :]).then_inc(stored[i], 16)

            def wide(c, i, again=True):
                step(c, i, c * SLOTS + SLOTS, c * J, again)

            wide(0, 0, again=False)
            wide(1, 1, again=False)
            with act.Fori(1, (CHUNKS - 2) // 2) as t:
                for i in range(2):
                    wide(t * 2 + i, i)
            wide(CHUNKS - 2, 0)
            for m in range(NARROW):
                c = CHUNKS - 1 + m
                used = (CHUNKS - 1) * SLOTS + (m + 1) * LAST_SLOTS
                if c == FINAL:
                    used += len(TAIL_PARTS) - 1
                step(c, c % 2, used, NB - J + m * LAST_J, nj=LAST_J)
            for i in range(2):
                act.wait_ge(stored[i], 16 * ((FINAL + 2 - i) // 2))

        @block.vector
        def _(dve):
            def quarter(q):
                return slice(q * XB, q * XB + XB)

            def centre(out, in_, q, which, ready):
                n = which * XQ + q + 1
                nc.vector.reduce_sum(node_sum[:, which, quarter(q)], in_[:, quarter(q), :],
                                     AX_X).then_inc(node_sum_ready, 1)
                dve.wait_ge(node_sum_ready, n)
                sums = node_sum[:, which, quarter(q)].unsqueeze(2).to_broadcast([P, XB, D])
                nc.vector.scalar_tensor_tensor(out=out[:, quarter(q), :], in0=sums, scalar=-1.0 / D,
                                               in1=in_[:, quarter(q), :], op0=ALU.mult,
                                               op1=ALU.add).then_inc(ready, 1)

            for q in range(XQ):
                dve.wait_ge(x_in[q], 32)
                nc.vector.scalar_tensor_tensor(out=u_sb[:, quarter(q), :], in0=u_sb[:, quarter(q), :], scalar=P_DROP,
                                               in1=x_sb[:, quarter(q), :], op0=ALU.is_ge,
                                               op1=ALU.mult).then_inc(masked, 1)
                dve.wait_ge(masked, q + 1)
                centre(xdrop, u_sb, q, 0, dropped)
            for q in range(XQ):
                centre(x_sb, x_sb, q, 1, x_centred)
            dve.wait_ge(x_centred, XQ)

            def normalise(c, i, block0, stores=None, nj=J):
                def per_row(v):
                    return v[:, 0:nj].unsqueeze(2).to_broadcast([P, nj, D])

                dve.wait_ge(folded_ready, c + 1)
                nc.vector.scalar_tensor_tensor(out=y[:, i, 0:nj, :], in0=folded[i][:, 0:nj, :],
                                               scalar=1.0 / (1.0 - P_DROP), in1=x_sb[:, bass.ds(block0, nj), :],
                                               op0=ALU.mult, op1=ALU.add).then_inc(y_ready, 1)
                dve.wait_ge(y_ready, c + 1)
                nc.vector.tensor_tensor(squares[:, 0:nj, :], y[:, i, 0:nj, :], y[:, i, 0:nj, :],
                                        ALU.mult).then_inc(squares_ready, 1)
                dve.wait_ge(squares_ready, c + 1)
                nc.vector.reduce_sum(square_sum[:, 0:nj], squares[:, 0:nj, :], AX_X).then_inc(var_ready, 1)
                dve.wait_ge(std_ready, c + 1)
                nc.vector.reciprocal(rstd[:, 0:nj], std[:, 0:nj]).then_inc(rstd_ready, 1)
                if stores is not None:
                    dve.wait_ge(stored[i], stores)
                dve.wait_ge(rstd_ready, c + 1)
                nc.vector.tensor_tensor(rows[:, i, 0:nj, :], y[:, i, 0:nj, :], per_row(rstd),
                                        ALU.mult).then_inc(rows_ready, 1)
                dve.wait_ge(rows_ready, c + 1)

            normalise(0, 0, 0)
            normalise(1, 1, J)
            with dve.Fori(1, (CHUNKS - 2) // 2) as t:
                for i in range(2):
                    c = t * 2 + i
                    normalise(c, i, c * J, stores=t * 16)
            normalise(CHUNKS - 2, 0, (CHUNKS - 2) * J, stores=16 * ((CHUNKS - 2) // 2))
            for m in range(NARROW):
                c = CHUNKS - 1 + m
                normalise(c, c % 2, NB - J + m * LAST_J, stores=16 * (c // 2), nj=LAST_J)


def kernel(x, adj, L0_gnn_u):
    import numpy as np
    import concourse.bacc as bacc
    from concourse.bass_utils import run_bass_kernel_spmd

    nc = bacc.Bacc("TRN2", target_bir_lowering=False, num_devices=1)
    fp32 = mybir.dt.float32
    a = np.asarray(adj).reshape(P, CHUNKS, J, P, SLOTS, PB)[:, :CHUNKS - 1].transpose(1, 4, 3, 5, 2, 0)
    z = np.asarray(adj).reshape(P, CHUNKS, NARROW, LAST_J, P, LAST_SLOTS, LAST_PB)[:, -1].transpose(1, 4, 3, 5, 2, 0)
    arrays = {
        "x": np.ascontiguousarray(x).reshape(P, NB, D),
        "adj": np.ascontiguousarray(a).reshape((CHUNKS - 1) * SLOTS, P, PB, COLS),
        "adj_last": np.ascontiguousarray(z).reshape(SLOTS, P, LAST_PB, LAST_COLS),
        "u": np.ascontiguousarray(L0_gnn_u).reshape(P, NB, D),
    }
    args = [nc.dram_tensor(n, v.shape, fp32, kind="ExternalInput").ap() for n, v in arrays.items()]
    out = nc.dram_tensor("out", (P, NB, D), fp32, kind="ExternalOutput").ap()
    graph_layernorm(nc, *args, out)
    r = run_bass_kernel_spmd(nc, [arrays], core_ids=[0])
    return r.results[0]["out"].reshape(N, D)
```
